# Optimizing a Trainium2 kernel written in Bass

```python
import numpy as np
import jax
import jax.numpy as jnp

def _softmax(x, axis=-1):
    return jax.nn.softmax(x, axis=axis)

def _gelu(x):
    return jax.nn.gelu(x, approximate=True)

def _silu(x):
    return jax.nn.silu(x)

def _sigmoid(x):
    return jax.nn.sigmoid(x)

def _layernorm(x, axis=-1, eps=1e-05):
    m = jnp.mean(x, axis=axis, keepdims=True)
    v = jnp.var(x, axis=axis, keepdims=True)
    return (x - m) / jnp.sqrt(v + eps)

def _scatter_add(tgt, idx, src, axis=0):
    return tgt.at[idx].add(src)

def _segment_sum(src, seg, n):
    return jax.ops.segment_sum(src, seg, n)
kernel_name = 'mk_sandwich_d1_jaxref_r2_46a774'

def setup_inputs(seed: int=0):
    np.random.seed(seed)
    _w = jnp.asarray

    def _L0_attn_setup():
        import jax, jax.numpy as jnp
        import numpy as np
        from jax import lax
        B, T, D, H = (4, 2048, 512, 16)
        d = D // H
        key = jax.random.key(seed)
        k0, k1, k2, k3, k4 = jax.random.split(key, 5)
        s = 1.0 / np.sqrt(D)
        x = jax.random.normal(k0, (B, T, D), dtype=jnp.float32)
        Wv = jax.random.normal(k1, (D, D), dtype=jnp.float32) * s
        Wo = jax.random.normal(k2, (D, D), dtype=jnp.float32) * s
        Wg = jax.random.normal(k3, (H, D), dtype=jnp.float32) * s
        Wb = jax.random.normal(k4, (H, D), dtype=jnp.float32) * s
        return {'x': x, 'Wv': Wv, 'Wo': Wo, 'Wg': Wg, 'Wb': Wb}
    _L0_attn_in = _L0_attn_setup()

    def _L0_ffn_setup():
        import jax, jax.numpy as jnp
        import numpy as np
        LN_EPS = 0.001
        EPS = 1e-05
        QB = 128.0

        def ste_round(x):
            return x + jax.lax.stop_gradient(jnp.round(x) - x)
        key = jax.random.key(seed)
        k1, k2 = jax.random.split(key)
        x = jax.random.normal(k1, (4, 4096, 512), dtype=jnp.float32)
        weight = jax.random.normal(k2, (512, 512), dtype=jnp.float32) * 0.02
        ln_gamma = jnp.ones((512,), dtype=jnp.float32)
        ln_beta = jnp.zeros((512,), dtype=jnp.float32)
        return {'x': x, 'weight': weight, 'ln_gamma': ln_gamma, 'ln_beta': ln_beta}
    _L0_ffn_in = _L0_ffn_setup()
    _d = {'L0_attn_x': _L0_attn_in['x'], 'L0_attn_Wv': _L0_attn_in['Wv'], 'L0_attn_Wo': _L0_attn_in['Wo'], 'L0_attn_Wg': _L0_attn_in['Wg'], 'L0_attn_Wb': _L0_attn_in['Wb'], 'L0_ffn_weight': _L0_ffn_in['weight'], 'L0_ffn_ln_gamma': _L0_ffn_in['ln_gamma'], 'L0_ffn_ln_beta': _L0_ffn_in['ln_beta']}
    _x0 = _d['L0_attn_x']
    _d['L0_attn_x'] = jax.random.normal(jax.random.fold_in(jax.random.key(seed), 1), (4, 4096, 512), dtype=_x0.dtype)
    del _x0
    return _d

def reference(L0_attn_x, L0_attn_Wv, L0_attn_Wo, L0_attn_Wg, L0_attn_Wb, L0_ffn_weight, L0_ffn_ln_gamma, L0_ffn_ln_beta):

    def _L0_attn_ref(x, Wv, Wo, Wg, Wb):
        import jax, jax.numpy as jnp
        import numpy as np
        from jax import lax
        B, T, D, H = (4, 2048, 512, 16)
        d = D // H
        Bb, Tt, Dd = x.shape
        dd = Dd // H
        rk = x.reshape(Bb, Tt, H, dd)
        rk = rk / jnp.maximum(jnp.linalg.norm(rk, axis=-1, keepdims=True), 1e-12)
        wk = jnp.pad(rk[:, :-1], ((0, 0), (1, 0), (0, 0), (0, 0)))
        v = (x @ Wv.T).reshape(Bb, Tt, H, dd)
        gate = jax.nn.sigmoid(x @ Wg.T)
        beta = jax.nn.sigmoid(x @ Wb.T)

        def step(S, inp):
            rk_t, wk_t, v_t, g_t, b_t = inp
            pred = jnp.einsum('bhk,bhkd->bhd', wk_t, S)
            err = (v_t - pred) * b_t[..., None]
            S = S + wk_t[..., None] * err[..., None, :]
            o = jnp.einsum('bhk,bhkd->bhd', rk_t, S) * g_t[..., None]
            return (S, o)
        to_time = lambda a: jnp.moveaxis(a, 1, 0)
        xs = (to_time(rk), to_time(wk), to_time(v), to_time(gate), to_time(beta))
        S0 = jnp.zeros((Bb, H, dd, dd), x.dtype)
        _, out = lax.scan(step, S0, xs)
        out = jnp.moveaxis(out, 0, 1).reshape(Bb, Tt, Dd)
        return out @ Wo.T

    def _L0_ffn_ref(x, weight, ln_gamma, ln_beta):
        import jax, jax.numpy as jnp
        import numpy as np
        LN_EPS = 0.001
        EPS = 1e-05
        QB = 128.0

        def ste_round(x):
            return x + jax.lax.stop_gradient(jnp.round(x) - x)
        mu = jnp.mean(x, axis=-1, keepdims=True)
        var = jnp.var(x, axis=-1, keepdims=True)
        xn = (x - mu) * jax.lax.rsqrt(var + LN_EPS) * ln_gamma + ln_beta
        beta = jnp.mean(jnp.abs(weight))
        w_q = jnp.clip(ste_round(weight / (beta + EPS)), -1.0, 1.0)
        gamma = jnp.max(jnp.abs(xn))
        xq = jnp.clip(xn * QB / gamma, -QB + EPS, QB - EPS)
        y = jnp.einsum('bsd,du->bsu', xq, w_q)
        return y * (gamma * beta / QB)
    x = L0_attn_x
    x = x + _layernorm(_L0_attn_ref(_layernorm(x, axis=-1), L0_attn_Wv, L0_attn_Wo, L0_attn_Wg, L0_attn_Wb), axis=-1)
    x = x + _layernorm(_L0_ffn_ref(_layernorm(x, axis=-1), L0_ffn_weight, L0_ffn_ln_gamma, L0_ffn_ln_beta), axis=-1)
    return x

_drawn_inputs = setup_inputs


def setup_inputs(seed=0):
    import zlib

    import numpy as np

    out = dict(_drawn_inputs(seed))
    spreads = {'L0_ffn_ln_gamma': (1.0, 0.2), 'L0_ffn_ln_beta': (0.0, 0.1)}
    factors = {}
    for name, (base, spread) in spreads.items():
        noise = np.random.default_rng([zlib.crc32(name.encode()), seed]).standard_normal(out[name].shape)
        drawn = base * np.exp(spread * noise) if base else spread * noise
        out[name] = jnp.asarray(drawn.astype(out[name].dtype))
    for name, factor in factors.items():
        out[name] = (out[name] * factor).astype(out[name].dtype)
    return out
```

```python
from contextlib import ExitStack

import concourse.bass as bass
from concourse import mybir

ALU = mybir.AluOpType
ACT = mybir.ActivationFunctionType
AX_X = mybir.AxisListType.X
F32 = mybir.dt.float32
F16 = mybir.dt.float16
I32 = mybir.dt.int32
RMAX = bass.bass_isa.ReduceOp.max
RADD = bass.bass_isa.ReduceOp.add

P = 128
B, T, D, H = 4, 4096, 512, 16
HD = D // H
C = P // B
KB = D // P
NT = T // C
BODY = 8
HALF = C // 2
LN_EPS = 1e-5
FFN_LN_EPS = 1e-3
QB, Q_EPS = 128.0, 1e-5
NORM2_MIN = 1e-24
LN_SHIFT = 40
G = 4
NG = NT // G

PARTS3 = ((0, 0), (0, 1), (1, 0))


def setup(nc, io, k):
    with ExitStack() as ctx:
        def sb(name, shape, dt=F32):
            return ctx.enter_context(nc.sbuf_tensor(name, shape, dt))

        def sem(name):
            return ctx.enter_context(nc.semaphore(name))

        raw = {n: sb(f"raw_{n}", [P, KB, D]) for n in ("v", "o", "f")}
        raw_g = sb("raw_g", [2 * H, D])
        gb_rows = sb("gb_rows", [2 * KB, P])
        wt = {n: sb(f"wt_{n}", [P, KB, D]) for n in ("v", "o")}
        wt_g = sb("wt_g", [P, KB, 2 * H])
        top = sb("top", [P, 4])
        top_all = sb("top_all", [P, 4])
        top_floor = sb("top_floor", [P, 4])
        pow2 = sb("pow2", [P, 4])
        unit = sb("unit", [P, 4])
        down = sb("down", [P, 4])
        attn_down = sb("attn_down", [P, 1])
        thr = sb("thr", [P, 2])
        above = sb("above", [P, KB, D])
        below = sb("below", [P, KB, D])
        banks = [ctx.enter_context(nc.psum_tensor(f"sbank{i}", [P, D], F32)) for i in range(2)]

        names = ("v", "o", "g", "f")
        loaded = {n: sem(f"w_loaded_{n}") for n in names + ("rows", "bc")}
        ident_s, mask_s, pad_s, shift_s = sem("ident_s"), sem("mask_s"), sem("pad_s"), sem("shift_s")
        top_s, all_s, scale_s, thr_s = sem("top_s"), sem("all_s"), sem("scale_s"), sem("thr_s")
        turned, scaled, hi_s, lo_s = sem("turned"), sem("scaled"), sem("hi_s"), sem("lo_s")
        cmp_s, wq_s, rows_s = sem("cmp_s"), sem("wq_s"), sem("rows_s")

        turns = [(n, kb) for n in ("v", "o") for kb in range(KB)]

        block = ctx.enter_context(nc.Block())

        @block.sync
        def _(sp):
            for n, src in (("v", io["Wv"]), ("o", io["Wo"]), ("f", io["Wf"])):
                sp.dma_start(raw[n][:, :, :], src.rearrange("(k p) n -> p k n", p=P)).then_inc(loaded[n], 16)
            sp.dma_start(raw_g[0:H, :], io["Wb"]).then_inc(loaded["g"], 16)
            sp.dma_start(raw_g[H:2 * H, :], io["Wg"]).then_inc(loaded["g"], 16)
            sp.dma_start(gb_rows[0:KB, :], io["gamma"].rearrange("(k p) -> k p", p=P)).then_inc(loaded["rows"], 16)
            sp.dma_start(gb_rows[KB:2 * KB, :], io["beta"].rearrange("(k p) -> k p", p=P)).then_inc(loaded["rows"], 16)
            for dst, src in ((k["gamma_bc"], io["gamma"]), (k["beta_bc"], io["beta"])):
                sp.dma_start(dst[:, :], src.rearrange("(a n) -> a n", a=1).to_broadcast([P, D])).then_inc(loaded["bc"], 16)
            sp.wait_ge(loaded["bc"], 32)

        @block.gpsimd
        def _(pool):
            pool.memset(k["ident"][:, :], 0.0).then_inc(ident_s, 1)
            pool.memset(k["neg_mask"][:, :], -1.0).then_inc(mask_s, 1)
            pool.memset(k["neg_half"][:, :], -0.5)
            pool.memset(k["minus_one"][:, :], -1.0)
            pool.memset(k["ln_eps"][:, :], LN_EPS)
            pool.memset(k["z_gain"][:, :], 1.0 + FFN_LN_EPS)
            pool.memset(k["z_eps"][:, :], LN_EPS * FFN_LN_EPS)
            pool.memset(k["rn_bias"][:, :], LN_SHIFT / 2 * 0.6931471805599453)
            pool.memset(k["shift"][:, :], 0.0).then_inc(ident_s, 1)
            pool.memset(k["carry"][:, :], 0.0).then_inc(ident_s, 1)
            pool.wait_ge(ident_s, 3)
            pool.affine_select(out=k["ident"][:, :], in_=k["ident"][:, :], compare_op=ALU.not_equal, fill=1.0,
                               base=0, pattern=[[-1, P]], channel_multiplier=1).then_inc(ident_s, 1)
            pool.wait_ge(ident_s, 4)
            pool.affine_select(out=k["shift"][:, :], in_=k["shift"][:, :], compare_op=ALU.not_equal, fill=1.0,
                               base=-1, pattern=[[1, P]], channel_multiplier=-1).then_inc(shift_s, 1)
            pool.wait_ge(shift_s, 1)
            firsts = k["carry"][:, 0:P:C]
            pool.affine_select(out=firsts, in_=firsts, compare_op=ALU.not_equal, fill=1.0,
                               base=1 - C, pattern=[[-C, B]], channel_multiplier=1).then_inc(shift_s, 1)
            pool.wait_ge(shift_s, 2)
            pool.memset(k["shift"][:, 0:P:C], 0.0).then_inc(mask_s, 1)
            pool.wait_ge(mask_s, 2)
            for b in range(B):
                m = k["neg_mask"][C * b:C * b + C, :]
                pool.affine_select(out=m, in_=m, compare_op=ALU.is_gt, fill=0.0, base=0,
                                   pattern=[[1, C]], channel_multiplier=-1).then_inc(mask_s, 1)
                pool.wait_ge(mask_s, 3 + b)
            pool.wait_ge(top_s, 5)
            pool.partition_all_reduce(top_all[:, 0:3], top[:, 0:3], P, RMAX).then_inc(all_s, 1)
            pool.partition_all_reduce(top_all[:, 3:4], top[:, 3:4], P, RADD).then_inc(all_s, 1)

        @block.tensor
        def _(pe):
            pe.wait_ge(ident_s, 4)
            for n, (name, kb) in enumerate(turns):
                if kb == 0:
                    pe.wait_ge(loaded[name], 16)
                if n >= 2:
                    pe.wait_ge(scaled, n - 1)
                for ob in range(KB):
                    last = pe.transpose(banks[n % 2][:, P * ob:P * ob + P],
                                        raw[name][:, ob, P * kb:P * kb + P], k["ident"][:, :])
                last.then_inc(turned, 1)
            pe.wait_ge(loaded["g"], 32)
            pe.wait_ge(scaled, len(turns))
            for kb in range(KB):
                last = pe.transpose(banks[0][:, 2 * H * kb:2 * H * kb + 2 * H],
                                    raw_g[:, P * kb:P * kb + P], k["ident"][0:2 * H, 0:2 * H])
            last.then_inc(turned, 1)
            pe.wait_ge(loaded["rows"], 32)
            pe.transpose(banks[1][:, 0:2 * KB], gb_rows[:, :], k["ident"][0:2 * KB, 0:2 * KB]).then_inc(turned, 1)

        @block.scalar
        def _(act):
            act.wait_ge(scale_s, 4)
            for n, (name, kb) in enumerate(turns):
                act.wait_ge(turned, n + 1)
                c = names.index(name)
                nc.scalar.activation(wt[name][:, kb, :], banks[n % 2][:, :], ACT.Identity,
                                     scale=down[:, c:c + 1]).then_inc(scaled, 1)
            act.wait_ge(turned, len(turns) + 1)
            nc.scalar.activation(wt_g[:, :, :].rearrange("p k n -> p (k n)"), banks[0][:, 0:KB * 2 * H], ACT.Identity,
                                 scale=down[:, 2:3]).then_inc(scaled, 1)
            act.wait_ge(turned, len(turns) + 2)
            nc.scalar.activation(k["gb_cols"][:, :], banks[1][:, 0:2 * KB], ACT.Copy).then_inc(rows_s, 1)
            act.wait_ge(rows_s, 1)

        @block.vector
        def _(dve):
            for c, n in enumerate(("v", "o")):
                dve.wait_ge(loaded[n], 16)
                dve.tensor_reduce(top[:, c:c + 1], raw[n][:, :, :].rearrange("p k n -> p (k n)"), AX_X, ALU.max,
                                  apply_absolute_value=True).then_inc(top_s, 1)
            dve.memset(top[:, 2:3], 0.0).then_inc(pad_s, 1)
            dve.wait_ge(pad_s, 1)
            dve.wait_ge(loaded["g"], 32)
            dve.tensor_reduce(top[0:2 * H, 2:3], raw_g[:, :], AX_X, ALU.max, apply_absolute_value=True).then_inc(top_s, 2)
            dve.wait_ge(loaded["f"], 16)
            dve.tensor_reduce(top[:, 3:4], raw["f"][:, :, :].rearrange("p k n -> p (k n)"), AX_X, ALU.add,
                              apply_absolute_value=True).then_inc(top_s, 1)
            dve.wait_ge(all_s, 2)
            dve.tensor_scalar(top_floor[:, :], top_all[:, :], 1e-30, None, ALU.max).then_inc(scale_s, 1)
            dve.wait_ge(scale_s, 1)
            dve.tensor_scalar(pow2[:, :].bitcast(I32), top_floor[:, :].bitcast(I32), 0x7F800000, None,
                              ALU.bitwise_and).then_inc(scale_s, 1)
            dve.wait_ge(scale_s, 2)
            dve.tensor_scalar(unit[:, :], pow2[:, :], 2.0, None, ALU.mult).then_inc(scale_s, 1)
            dve.wait_ge(scale_s, 3)
            dve.reciprocal(down[:, :], unit[:, :]).then_inc(scale_s, 1)
            dve.wait_ge(scale_s, 4)
            dve.tensor_tensor(attn_down[:, :], down[:, 0:1], down[:, 1:2], ALU.mult).then_inc(scale_s, 1)
            dve.wait_ge(scale_s, 5)
            dve.scalar_tensor_tensor(out=k["attn_eps"][:, :], in0=attn_down[:, :], scalar=LN_EPS, in1=attn_down[:, :],
                                     op0=ALU.mult, op1=ALU.mult)
            dve.tensor_scalar(k["gate_unit"][:, :], unit[:, 2:3], -1.0, None, ALU.mult)
            dve.tensor_scalar(k["w_mean"][:, :], top_all[:, 3:4], 1.0 / (D * D), None, ALU.mult).then_inc(thr_s, 1)
            dve.wait_ge(thr_s, 1)
            dve.tensor_scalar(thr[:, 0:1], k["w_mean"][:, :], Q_EPS, 0.5, ALU.add, ALU.mult).then_inc(thr_s, 1)
            dve.tensor_scalar(thr[:, 1:2], k["w_mean"][:, :], Q_EPS, -0.5, ALU.add, ALU.mult).then_inc(thr_s, 1)
            dve.wait_ge(thr_s, 3)
            dve.tensor_scalar(above[:, :, :], raw["f"][:, :, :], thr[:, 0:1], None, ALU.is_gt).then_inc(cmp_s, 1)
            dve.tensor_scalar(below[:, :, :], raw["f"][:, :, :], thr[:, 1:2], None, ALU.is_lt).then_inc(cmp_s, 1)
            dve.wait_ge(cmp_s, 2)
            dve.tensor_tensor(k["wq"][:, :, :], above[:, :, :], below[:, :, :], ALU.subtract).then_inc(wq_s, 1)
            dve.wait_ge(scaled, len(turns) + 1)
            pairs = ((k["wv"], wt["v"]), (k["wo"], wt["o"]), (k["wgb"], wt_g))
            for parts, full in pairs:
                dve.tensor_copy(parts[:, 0, :, :], full[:, :, :]).then_inc(hi_s, 1)
            for n, (parts, full) in enumerate(pairs):
                dve.wait_ge(hi_s, n + 1)
                dve.tensor_tensor(parts[:, 1, :, :], full[:, :, :], parts[:, 0, :, :], ALU.subtract).then_inc(lo_s, 1)
            dve.wait_ge(lo_s, 3)
            dve.wait_ge(wq_s, 1)


LAG_LOAD = 10
LAG_STATS = 9
LAG_XHAT = 8
LAG_TURN = 7
LAG_NORM = 6
LAG_V = 5
LAG_GRAM = 4
LAG_OUT = -1
LAG_RES = -2
LAG_STATS2 = -3
LAG_Z = -4
LAG_XN = -5
LAG_MAX = -6
FIRST, LAST = -LAG_LOAD, NT - 1 - LAG_MAX


def attention(nc, io, k):
    with ExitStack() as ctx:
        def sb(name, shape, dt=F32):
            return ctx.enter_context(nc.sbuf_tensor(name, shape, dt))

        def bank(name):
            return ctx.enter_context(nc.psum_tensor(name, [P, D], F32))

        def sem(name):
            return ctx.enter_context(nc.semaphore(name))

        x_in = sb("x_in", [P, 4, D])
        x_res = sb("x_res", [P, 4, D])
        ln_raw = sb("ln_raw", [P, 6])
        ln_mv = sb("ln_mv", [P, 2, 2])
        ln_sc = sb("ln_sc", [P, 2, 4])
        x_hat = sb("x_hat", [P, 4, D])
        x_sq = sb("x_sq", [P, 2, D])
        xt = sb("xt", [P, 4, 2, KB, P], F16)
        ss = sb("ss", [P, 2, H])
        ss_raw = sb("ss_raw", [P, H])
        ss_ln = sb("ss_ln", [P, H])
        rn0 = sb("rn0", [P, 2, H])
        rn_t = sb("rn_t", [P, 2, H])
        rn = sb("rn", [P, 2, H])
        val = sb("val", [P, 8, D])
        g_exp = sb("g_exp", [P, 2, 2 * H])
        g_den = sb("g_den", [P, 2 * H])
        gates = sb("gates", [P, 8, 2 * H])
        gate = sb("gate", [P, 8, H])
        key = sb("key", [P, 2, D])
        key_t = sb("key_t", [P, 8, H, C])
        key_b = sb("key_b", [P, 8, D])
        b_mask = sb("b_mask", [P, 2, H, C])
        m_t = sb("m_t", [P, 2, H, C])
        sys = sb("sys", [P, C, C])
        prod = sb("prod", [P, HALF * HALF])
        t_t = sb("t_t", [P, 2, 2, H, C])
        rhs = sb("rhs", [P, 2, D])
        err = sb("err", [P, 2, D])
        state = sb("state", [P, 2, D])
        pred = sb("pred", [P, D])
        o_g = sb("o_g", [P, 2, D])
        ot = sb("ot", [P, 2, 2, KB, P], F16)
        y_raw = sb("y_raw", [P, 6])
        y_mv = sb("y_mv", [P, 2, 2])
        y_sc = sb("y_sc", [P, 2, 4])
        y_n = sb("y_n", [P, 2, D])
        x1 = sb("x1", [P, 4, D])
        z_raw = sb("z_raw", [P, 6])
        z_mv = sb("z_mv", [P, 2, 2])
        z_sc = sb("z_sc", [P, 2, 5])
        z = sb("z", [P, 2, D])
        xn_g = sb("xn_g", [P, D])
        xn = sb("xn", [P, 2, D])

        ps_xt, ps_ot, ps_v, ps_g = bank("ps_xt"), bank("ps_ot"), bank("ps_v"), bank("ps_g")
        ps_gram, ps_chain, ps_s, ps_y = bank("ps_gram"), bank("ps_chain"), bank("ps_s"), bank("ps_y")

        x_loaded = [sem(f"x_loaded{i}") for i in range(4)]
        res_loaded = [sem(f"res_loaded{i}") for i in range(4)]
        x1_stored = [sem(f"x1_stored{i}") for i in range(4)]
        names = """first_gate ln_sums ln_stats ln_veps ln_rstd ln_scale xhat_done sq_done xt_psum xt_hi xt_lo
            ss_sum ss_done ln_done rn0_done rn_sq rn_half rn_done v_psum g_psum v_done gexp_done gden_done gates_done gate_psum gate_done
            key_done keyt_done keyb_done bmask_done gram_psum mt_done
            sys_done diag_done elim_prod elim_done tt_done
            pred_psum rhs_done err_psum err_done s_psum state_done
            pred_done o_done ot_psum ot_hi ot_lo y_psum
            y_sums y_stats y_veps y_rstd y_scale yn_done x1_done
            z_sums z_stats z_gain z_veps z_rstd z_scale z_done z_kept xng_done xn_done max_done""".split()
        s = {n: sem(n) for n in names}

        def spread(a):
            return a.unsqueeze(2).to_broadcast([P, H, HD])

        def heads(a):
            return a.rearrange("p (h e) -> p h e", h=H)

        def on(base, step, lag):
            n = times(base, BODY, step + lag)
            return n, (step + lag) % BODY, not isinstance(n, int) or 0 <= n < NT

        def upto(count):
            return min(count, NT) if isinstance(count, int) else count

        def times(base, many, more):
            return more if base is None else base * many + more

        def wait(eng, semaphore, count):
            if not isinstance(count, int) or count > 0:
                eng.wait_ge(semaphore, count)

        def quads(base, step, lag):
            return times(base, BODY // 4, (step + lag) // 4)

        def run(eng, step):
            turns = (NT - LAG_LOAD) // BODY
            for j in range(FIRST, BODY):
                step(None, j)
            with eng.Fori(1, turns) as base:
                for i in range(BODY):
                    step(base, i)
            for j in range(turns * BODY, LAST + 1):
                step(None, j)

        def later(l, part):
            def at(ring):
                return xt[:, ring % 4, part, :, :].rearrange("p k (b t) -> p k b t", b=B)
            return (at(l + 3)[:, :, :, C - 1:C], at(l)[:, :, :, 0:C - 1],
                    ps_xt[:, :].rearrange("p (k b t) -> p k b t", k=KB, b=B))

        block = ctx.enter_context(nc.Block())

        def rows(t, base, step, lag):
            return t[:, bass.ds(times(base, BODY * C, (step + lag) * C), C), :]

        def tile(t, ring):
            return t[:, ring, :]

        @block.sync
        def _(sp):
            def step(base, j):
                n, l, live = on(base, j, LAG_LOAD)
                if live:
                    wait(sp, s["xhat_done"], n - 3)
                    wait(sp, s["sq_done"], n - 3)
                    wait(sp, s["ln_sums"], n - 3)
                    sp.dma_start(tile(x_in, l % 4), rows(io["x"], base, j, LAG_LOAD)).then_inc(x_loaded[l % 4], 16)
                n, l, live = on(base, j, 0)
                if live:
                    wait(sp, s["x1_done"], n - 3)
                    sp.dma_start(tile(x_res, l % 4), rows(io["x"], base, j, 0)).then_inc(res_loaded[l % 4], 16)
                n, l, live = on(base, j, LAG_STATS2)
                if live:
                    wait(sp, s["x1_done"], n + 1)
                    sp.dma_start(k["x1_dram"][bass.ds(n, 1), :, :].rearrange("a p d -> (a p) d"),
                                 x1[:, l % 4, :]).then_inc(x1_stored[l % 4], 16)
            run(sp, step)
            for i in range(4):
                sp.wait_ge(x1_stored[i], 16 * NT // 4)

        @block.gpsimd
        def _(pool):
            pool.memset(state[:, 0, :], 0.0).then_inc(s["state_done"], 1)
            pool.memset(gates[:, BODY - 1, :], 0.0).then_inc(s["first_gate"], 1)

            def step(base, j):
                n, l, live = on(base, j, LAG_XHAT)
                if live:
                    wait(pool, s["ln_stats"], n + 1)
                    wait(pool, s["xhat_done"], n - 1)
                    wait(pool, s["sq_done"], n - 1)
                    mv, sc = ln_mv[:, l % 2, :], ln_sc[:, l % 2, :]
                    pool.tensor_tensor(sc[:, 2:3], mv[:, 1:2], k["ln_eps"][:, :], ALU.add).then_inc(s["ln_veps"], 1)
                    pool.tensor_tensor(sc[:, 3:4], mv[:, 0:1], k["minus_one"][:, :], ALU.mult).then_inc(s["ln_veps"], 1)
                    wait(pool, s["ln_veps"], n * 2 + 2)
                    pool.tensor_tensor(sc[:, 0:1], sc[:, 2:3], k["neg_half"][:, :], ALU.pow).then_inc(s["ln_rstd"], 1)
                    wait(pool, s["ln_rstd"], n + 1)
                    pool.tensor_tensor(sc[:, 1:2], sc[:, 3:4], sc[:, 0:1], ALU.mult).then_inc(s["ln_scale"], 1)
                n, l, live = on(base, j, LAG_RES)
                if live:
                    wait(pool, s["y_stats"], n + 1)
                    wait(pool, s["yn_done"], n - 1)
                    mv, sc = y_mv[:, l % 2, :], y_sc[:, l % 2, :]
                    pool.tensor_tensor(sc[:, 2:3], mv[:, 1:2], k["attn_eps"][:, :], ALU.add).then_inc(s["y_veps"], 1)
                    pool.tensor_tensor(sc[:, 3:4], mv[:, 0:1], k["minus_one"][:, :], ALU.mult).then_inc(s["y_veps"], 1)
                    wait(pool, s["y_veps"], n * 2 + 2)
                    pool.tensor_tensor(sc[:, 0:1], sc[:, 2:3], k["neg_half"][:, :], ALU.pow).then_inc(s["y_rstd"], 1)
                    wait(pool, s["y_rstd"], n + 1)
                    pool.tensor_tensor(sc[:, 1:2], sc[:, 3:4], sc[:, 0:1], ALU.mult).then_inc(s["y_scale"], 1)
                n, l, live = on(base, j, LAG_Z)
                if live:
                    wait(pool, s["z_stats"], n + 1)
                    wait(pool, s["z_done"], n - 1)
                    mv, sc = z_mv[:, l % 2, :], z_sc[:, l % 2, :]
                    pool.tensor_tensor(sc[:, 2:3], mv[:, 1:2], k["z_gain"][:, :], ALU.mult).then_inc(s["z_gain"], 1)
                    pool.tensor_tensor(sc[:, 3:4], mv[:, 0:1], k["minus_one"][:, :], ALU.mult).then_inc(s["z_veps"], 1)
                    wait(pool, s["z_gain"], n + 1)
                    pool.tensor_tensor(sc[:, 4:5], sc[:, 2:3], k["z_eps"][:, :], ALU.add).then_inc(s["z_veps"], 1)
                    wait(pool, s["z_veps"], n * 2 + 2)
                    pool.tensor_tensor(sc[:, 0:1], sc[:, 4:5], k["neg_half"][:, :], ALU.pow).then_inc(s["z_rstd"], 1)
                    wait(pool, s["z_rstd"], n + 1)
                    pool.tensor_tensor(sc[:, 1:2], sc[:, 3:4], sc[:, 0:1], ALU.mult).then_inc(s["z_scale"], 1)
                    wait(pool, s["z_scale"], n + 1)
                    pool.tensor_copy(k["z_scale"][:, bass.ds(n * 2, 2)], sc[:, 0:2]).then_inc(s["z_kept"], 1)
                n, l, live = on(base, j, LAG_GRAM)
                if live:
                    wait(pool, s["gates_done"], n + 1)
                    wait(pool, s["mt_done"], n - 1)
                    wait(pool, s["s_psum"], n - 7)
                    beta = gates[:, l, 0:H]
                    pool.tensor_tensor(b_mask[:, l % 2, :, :], spread(beta),
                                       k["neg_mask"][:, :].unsqueeze(1).to_broadcast([P, H, C]), ALU.mult).then_inc(s["bmask_done"], 1)
                    pool.tensor_tensor(heads(key_b[:, l, :]), heads(key[:, l % 2, :]), spread(beta),
                                       ALU.mult).then_inc(s["keyb_done"], 1)
                n, l, live = on(base, j, LAG_V)
                if live:
                    wait(pool, s["rn_done"], n + 1)
                    wait(pool, s["keyt_done"], n - 1)
                    wait(pool, s["keyb_done"], n - 1)
                    pool.tensor_tensor(heads(key[:, l % 2, :]), heads(x_hat[:, l % 4, :]), spread(rn[:, l % 2, :]),
                                       ALU.mult).then_inc(s["key_done"], 1)
                n, l, live = on(base, j, 0)
                if live:
                    wait(pool, s["err_done"], n + 1)
                    wait(pool, s["o_done"], n)
                    pool.tensor_tensor(pred[:, :], val[:, l, :], err[:, l % 2, :], ALU.subtract).then_inc(s["pred_done"], 1)
                    wait(pool, s["pred_done"], n + 1)
                    wait(pool, s["ot_psum"], n - 1)
                    wait(pool, s["gate_done"], n + 1)
                    pool.tensor_tensor(heads(o_g[:, l % 2, :]), heads(pred[:, :]), spread(gate[:, l, :]),
                                       ALU.mult).then_inc(s["o_done"], 1)
                n, l, live = on(base, j, LAG_XN)
                if live:
                    wait(pool, s["z_done"], n + 1)
                    wait(pool, s["xn_done"], n)
                    pool.tensor_tensor(xn_g[:, :], z[:, l % 2, :], k["gamma_bc"][:, :], ALU.mult).then_inc(s["xng_done"], 1)
                    wait(pool, s["xng_done"], n + 1)
                    wait(pool, s["max_done"], n - 1)
                    pool.tensor_tensor(xn[:, l % 2, :], xn_g[:, :], k["beta_bc"][:, :], ALU.add).then_inc(s["xn_done"], 1)
                n, l, live = on(base, j, LAG_RES)
                if live:
                    wait(pool, s["yn_done"], n + 1)
                    pool.wait_ge(res_loaded[l % 4], quads(base, j, LAG_RES) * 16 + 16)
                    if not isinstance(n, int) or n >= 4:
                        pool.wait_ge(x1_stored[l % 4], quads(base, j, LAG_RES) * 16)
                    wait(pool, s["z_sums"], n - 3)
                    wait(pool, s["z_done"], n - 3)
                    pool.tensor_tensor(x1[:, l % 4, :], y_n[:, l % 2, :], x_res[:, l % 4, :], ALU.add).then_inc(s["x1_done"], 1)
            run(pool, step)

        @block.scalar
        def _(act):
            def step(base, j):
                n, l, live = on(base, j, LAG_XHAT)
                if live:
                    wait(act, s["ln_scale"], n + 1)
                    act.wait_ge(x_loaded[l % 4], quads(base, j, LAG_XHAT) * 16 + 16)
                    wait(act, s["xt_psum"], n - 3)
                    wait(act, s["key_done"], n - 3)
                    sc = ln_sc[:, l % 2, :]
                    nc.scalar.activation(x_hat[:, l % 4, :], x_in[:, l % 4, :], ACT.Identity,
                                         scale=sc[:, 0:1], bias=sc[:, 1:2]).then_inc(s["xhat_done"], 1)
                    wait(act, s["ss_sum"], n - 1)
                    nc.scalar.activation(x_sq[:, l % 2, :], x_in[:, l % 4, :], ACT.Square,
                                         scale=sc[:, 0:1], bias=sc[:, 1:2]).then_inc(s["sq_done"], 1)
                n, l, live = on(base, j, LAG_TURN)
                if live:
                    wait(act, s["xt_psum"], n + 1)
                    wait(act, s["v_psum"], n - 3)
                    last, most, src = later(l, 0)
                    nc.scalar.activation(last, src[:, :, :, 0:1], ACT.Copy)
                    nc.scalar.activation(most, src[:, :, :, 1:C], ACT.Copy).then_inc(s["xt_hi"], 1)
                n, l, live = on(base, j, LAG_NORM)
                if live:
                    wait(act, s["ss_done"], n + 1)
                    wait(act, s["rn0_done"], n)
                    nc.scalar.activation(ss_ln[:, :], ss[:, l % 2, :], ACT.Ln, scale=float(2 ** LN_SHIFT)).then_inc(s["ln_done"], 1)
                    wait(act, s["ln_done"], n + 1)
                    wait(act, s["rn_done"], n - 1)
                    nc.scalar.activation(rn0[:, l % 2, :], ss_ln[:, :], ACT.Exp, scale=-0.5,
                                         bias=k["rn_bias"][:, 0:1]).then_inc(s["rn0_done"], 1)
                n, l, live = on(base, j, LAG_RES)
                if live:
                    wait(act, s["y_scale"], n + 1)
                    wait(act, s["x1_done"], n - 1)
                    sc = y_sc[:, l % 2, :]
                    nc.scalar.activation(y_n[:, l % 2, :], ps_y[:, :], ACT.Identity,
                                         scale=sc[:, 0:1], bias=sc[:, 1:2]).then_inc(s["yn_done"], 1)
                n, l, live = on(base, j, LAG_V)
                if live:
                    wait(act, s["g_psum"], n + 1)
                    wait(act, s["gden_done"], n - 1)
                    nc.scalar.activation(g_exp[:, l % 2, :], ps_g[:, 0:2 * H], ACT.Exp,
                                         scale=k["gate_unit"][:, 0:1]).then_inc(s["gexp_done"], 1)
                    wait(act, s["v_psum"], n + 1)
                    wait(act, s["o_done"], n - 7)
                    wait(act, s["rhs_done"], n - 7)
                    nc.scalar.activation(val[:, l, :], ps_v[:, :], ACT.Copy).then_inc(s["v_done"], 1)
                n, l, live = on(base, j, 0)
                if live:
                    wait(act, s["err_psum"], n + 1)
                    wait(act, s["o_done"], n - 1)
                    wait(act, s["s_psum"], n - 1)
                    nc.scalar.activation(err[:, l % 2, :], ps_chain[:, :], ACT.Copy).then_inc(s["err_done"], 1)
                n, l, live = on(base, j, LAG_GRAM)
                if live:
                    wait(act, s["gate_psum"], n + 1)
                    wait(act, s["o_done"], n - 7)
                    nc.scalar.activation(gate[:, l, :], ps_g[:, 2 * H:3 * H], ACT.Copy).then_inc(s["gate_done"], 1)
                n, l, live = on(base, j, LAG_OUT)
                if live:
                    wait(act, s["ot_psum"], n + 1)
                    wait(act, s["y_psum"], n - 1)
                    nc.scalar.activation(ot[:, l % 2, 0, :, :].rearrange("p k t -> p (k t)"), ps_ot[:, :],
                                         ACT.Copy).then_inc(s["ot_hi"], 1)
                n, l, live = on(base, j, LAG_Z)
                if live:
                    wait(act, s["z_scale"], n + 1)
                    wait(act, s["xng_done"], n - 1)
                    wait(act, s["x1_done"], n + 1)
                    sc = z_sc[:, l % 2, :]
                    nc.scalar.activation(z[:, l % 2, :], x1[:, l % 4, :], ACT.Identity,
                                         scale=sc[:, 0:1], bias=sc[:, 1:2]).then_inc(s["z_done"], 1)
                n, l, live = on(base, j, 0)
                if live:
                    wait(act, s["s_psum"], n + 1)
                    wait(act, s["pred_psum"], n)
                    nc.scalar.activation(state[:, (l + 1) % 2, :], ps_s[:, :], ACT.Copy).then_inc(s["state_done"], 1)
            nc.scalar.preload_act_table_set("natural_log_exp_and_others")
            run(act, step)

        @block.vector
        def _(dve):
            def pair(base, j):
                q = j // 2 + 1
                return times(base, BODY // 2, q), base is None and not 0 <= q < NT // 2, q % 2

            def solve(base, j, part):
                q, off, ring = pair(base, j)
                if off:
                    return
                first = j % 2 == 0
                if first and part == 0:
                    wait(dve, s["mt_done"], q * 2 + 2)
                    wait(dve, s["tt_done"], q)
                    dve.transpose(sys[:, :, :], m_t[:, :, :, :].rearrange("p a h i -> p i (a h)")).then_inc(s["sys_done"], 1)
                    dve.wait_ge(s["sys_done"], q + 1)
                    flat = sys[:, :, :].rearrange("p i k -> p (i k)")
                    dve.memset(flat[:, 0:C * C:C + 1], 1.0).then_inc(s["diag_done"], 1)
                    dve.wait_ge(s["diag_done"], q + 1)
                lo, hi = (1, HALF) if first else (HALF, C - 1)
                cut = [lo + (hi - lo) * i // 3 for i in range(4)]
                for c in range(cut[part], cut[part + 1]):
                    shape = [P, C - 1 - c, c]
                    dst = sys[:, c + 1:C, 0:c]
                    tmp = prod[:, 0:(C - 1 - c) * c].rearrange("p (i k) -> p i k", k=c)
                    wait(dve, s["elim_done"], q * (C - 2) + (c - 1))
                    dve.tensor_tensor(tmp, sys[:, c + 1:C, c:c + 1].to_broadcast(shape),
                                      sys[:, c:c + 1, 0:c].to_broadcast(shape), ALU.mult).then_inc(s["elim_prod"], 1)
                    dve.wait_ge(s["elim_prod"], q * (C - 2) + c)
                    dve.tensor_tensor(dst, dst, tmp, ALU.add).then_inc(s["elim_done"], 1)
                if not first and part == 2:
                    dve.wait_ge(s["elim_done"], q * (C - 2) + (C - 2))
                    wait(dve, s["err_psum"], q * 2 - 2)
                    dve.transpose(t_t[:, ring, :, :, :].rearrange("p a h i -> p i (a h)"), sys[:, :, :]).then_inc(s["tt_done"], 1)

            def step(base, j):
                n, l, live = on(base, j, 0)
                if live:
                    wait(dve, s["pred_psum"], n + 1)
                    wait(dve, s["v_done"], n + 1)
                    wait(dve, s["err_psum"], n - 1)
                    dve.tensor_tensor(rhs[:, l % 2, :], val[:, l, :], ps_chain[:, :], ALU.subtract).then_inc(s["rhs_done"], 1)
                n, l, live = on(base, j, LAG_RES)
                if live:
                    wait(dve, s["y_psum"], n + 1)
                    wait(dve, s["y_stats"], n)
                    dve.bn_stats(y_raw[:, :], ps_y[:, :]).then_inc(s["y_sums"], 1)
                    wait(dve, s["y_sums"], n + 1)
                    wait(dve, s["y_scale"], n - 1)
                n, l, live = on(base, j, LAG_GRAM)
                if live:
                    wait(dve, s["key_done"], n + 1)
                    wait(dve, s["pred_psum"], n - 7)
                    wait(dve, s["gram_psum"], n - 7)
                    dve.transpose(key_t[:, l, :, :], heads(key[:, l % 2, :])).then_inc(s["keyt_done"], 1)
                n, l, live = on(base, j, LAG_RES)
                if live:
                    dve.bn_aggr(y_mv[:, l % 2, :], y_raw[:, :]).then_inc(s["y_stats"], 1)
                n, l, live = on(base, j, LAG_TURN)
                if live:
                    wait(dve, s["xt_hi"], n + 1)
                    wait(dve, s["v_psum"], n - 3)
                    (last_hi, most_hi, src), (last, most, _) = later(l, 0), later(l, 1)
                    dve.tensor_tensor(last, src[:, :, :, 0:1], last_hi, ALU.subtract)
                    dve.tensor_tensor(most, src[:, :, :, 1:C], most_hi, ALU.subtract).then_inc(s["xt_lo"], 1)
                solve(base, j, 0)
                n, l, live = on(base, j, LAG_NORM)
                if live:
                    y, t = rn0[:, l % 2, :], rn_t[:, :, :]
                    wait(dve, s["rn0_done"], n + 1)
                    wait(dve, s["rn_half"], n)
                    dve.tensor_tensor(t[:, 0, :], y, y, ALU.mult).then_inc(s["rn_sq"], 1)
                    wait(dve, s["rn_sq"], n + 1)
                    wait(dve, s["rn_done"], n)
                    dve.scalar_tensor_tensor(out=t[:, 1, :], in0=t[:, 0, :], scalar=-0.5, in1=ss[:, l % 2, :],
                                             op0=ALU.mult, op1=ALU.mult).then_inc(s["rn_half"], 1)
                    wait(dve, s["rn_half"], n + 1)
                    wait(dve, s["key_done"], n - 1)
                    dve.scalar_tensor_tensor(out=rn[:, l % 2, :], in0=t[:, 1, :], scalar=1.5, in1=y,
                                             op0=ALU.add, op1=ALU.mult).then_inc(s["rn_done"], 1)
                n, l, live = on(base, j, LAG_TURN)
                if live:
                    wait(dve, s["sq_done"], n + 1)
                    wait(dve, s["ss_done"], n)
                    dve.tensor_reduce(ss_raw[:, :], heads(x_sq[:, l % 2, :]), AX_X, ALU.add).then_inc(s["ss_sum"], 1)
                    wait(dve, s["ss_sum"], n + 1)
                    wait(dve, s["ln_done"], n - 1)
                    wait(dve, s["rn_half"], n - 1)
                    dve.tensor_scalar(ss[:, l % 2, :], ss_raw[:, :], NORM2_MIN, None, ALU.max).then_inc(s["ss_done"], 1)
                n, l, live = on(base, j, LAG_OUT)
                if live:
                    wait(dve, s["ot_hi"], n + 1)
                    wait(dve, s["y_psum"], n - 1)
                    dve.tensor_tensor(ot[:, l % 2, 1, :, :].rearrange("p k t -> p (k t)"), ps_ot[:, :],
                                      ot[:, l % 2, 0, :, :].rearrange("p k t -> p (k t)"), ALU.subtract).then_inc(s["ot_lo"], 1)
                solve(base, j, 1)
                n, l, live = on(base, j, LAG_V)
                if live:
                    wait(dve, s["gexp_done"], n + 1)
                    wait(dve, s["gates_done"], n)
                    dve.tensor_scalar(g_den[:, :], g_exp[:, l % 2, :], 1.0, None, ALU.add).then_inc(s["gden_done"], 1)
                    wait(dve, s["gden_done"], n + 1)
                    wait(dve, s["gate_psum"], n - 6)
                    wait(dve, s["keyb_done"], n - 7)
                    dve.reciprocal(gates[:, l, :], g_den[:, :]).then_inc(s["gates_done"], 1)
                n, l, live = on(base, j, LAG_GRAM)
                if live:
                    wait(dve, s["gram_psum"], n + 1)
                    wait(dve, s["bmask_done"], n + 1)
                    wait(dve, s["sys_done"], times(base, BODY // 2, (j + LAG_GRAM) // 2))
                    flat = m_t[:, l % 2, :, :].rearrange("p h i -> p (h i)")
                    dve.tensor_tensor(flat, ps_gram[:, :], b_mask[:, l % 2, :, :].rearrange("p h i -> p (h i)"),
                                      ALU.mult).then_inc(s["mt_done"], 1)
                solve(base, j, 2)
                n, l, live = on(base, j, LAG_STATS2)
                if live:
                    wait(dve, s["x1_done"], n + 1)
                    wait(dve, s["z_stats"], n)
                    dve.bn_stats(z_raw[:, :], x1[:, l % 4, :]).then_inc(s["z_sums"], 1)
                n, l, live = on(base, j, LAG_STATS)
                if live:
                    dve.wait_ge(x_loaded[l % 4], quads(base, j, LAG_STATS) * 16 + 16)
                    wait(dve, s["ln_stats"], n)
                    dve.bn_stats(ln_raw[:, :], x_in[:, l % 4, :]).then_inc(s["ln_sums"], 1)
                    wait(dve, s["ln_sums"], n + 1)
                    wait(dve, s["ln_scale"], n - 1)
                n, l, live = on(base, j, LAG_STATS2)
                if live:
                    wait(dve, s["z_sums"], n + 1)
                    wait(dve, s["z_scale"], n - 1)
                n, l, live = on(base, j, LAG_MAX)
                if live:
                    wait(dve, s["xn_done"], n + 1)
                    dve.tensor_reduce(k["row_max"][:, bass.ds(n, 1)], xn[:, l % 2, :], AX_X, ALU.max,
                                      apply_absolute_value=True).then_inc(s["max_done"], 1)
                n, l, live = on(base, j, LAG_STATS2)
                if live:
                    dve.bn_aggr(z_mv[:, l % 2, :], z_raw[:, :]).then_inc(s["z_stats"], 1)
                n, l, live = on(base, j, LAG_STATS)
                if live:
                    dve.bn_aggr(ln_mv[:, l % 2, :], ln_raw[:, :]).then_inc(s["ln_stats"], 1)
            run(dve, step)

        @block.tensor
        def _(pe):
            def blocks():
                for h in range(H):
                    for b in range(B):
                        yield h, slice(C * b, C * b + C), slice(HD * h, HD * h + HD)

            def chain_ready(base, j):
                n, l, live = on(base, j, 0)
                if live:
                    wait(pe, s["state_done"], n + 1)
                    wait(pe, s["keyt_done"], n + 1)

            def error_ready(base, j):
                n, l, live = on(base, j, 0)
                if live:
                    wait(pe, s["tt_done"], times(base, BODY // 2, j // 2 + 1))
                    wait(pe, s["rhs_done"], n + 1)

            def gram_ready(base, j):
                n, l, live = on(base, j, LAG_GRAM)
                if live:
                    wait(pe, s["keyt_done"], n + 1)
                    wait(pe, s["mt_done"], n)

            def update_ready(base, j):
                n, l, live = on(base, j, 0)
                if live:
                    wait(pe, s["err_done"], n + 1)
                    wait(pe, s["keyb_done"], n + 1)

            def step(base, j):
                n, l, live = on(base, j, 0)
                if live:
                    if not on(base, j - 1, LAG_OUT)[2]:
                        chain_ready(base, j)
                    for h, q, e in blocks():
                        last = pe.matmul(ps_chain[q, e], key_t[q, l, h, :], state[q, l % 2, e], start=True, stop=True)
                    last.then_inc(s["pred_psum"], 1)
                n, l, live = on(base, j, LAG_TURN)
                if live:
                    wait(pe, s["xhat_done"], n + 1)
                    wait(pe, s["xt_lo"], n)
                    for kb in range(KB):
                        last = pe.transpose(ps_xt[:, P * kb:P * kb + P], x_hat[:, l % 4, P * kb:P * kb + P], k["ident"][:, :])
                    last.then_inc(s["xt_psum"], 1)
                n, l, live = on(base, j, LAG_V)
                if not live:
                    error_ready(base, j)
                if live:
                    wait(pe, s["xt_lo"], upto(n + 2))
                    wait(pe, s["gate_done"], n - 1)
                    wait(pe, s["gexp_done"], n)
                    for i in range(3 * KB):
                        kb, (a, w) = i // 3, PARTS3[i % 3]
                        last = pe.matmul(ps_g[:, 0:2 * H], xt[:, l % 4, a, kb, :], k["wgb"][:, w, kb, :],
                                         start=(i == 0), stop=(i == 3 * KB - 1))
                    last.then_inc(s["g_psum"], 1)
                    wait(pe, s["v_done"], n)
                    for i in range(3 * KB):
                        if i == 3 * KB - 1:
                            error_ready(base, j)
                        kb, (a, w) = i // 3, PARTS3[i % 3]
                        last = pe.matmul(ps_v[:, :], xt[:, l % 4, a, kb, :], k["wv"][:, w, kb, :],
                                         start=(i == 0), stop=(i == 3 * KB - 1))
                    last.then_inc(s["v_psum"], 1)
                n, l, live = on(base, j, 0)
                if live:
                    for h, q, e in blocks():
                        last = pe.matmul(ps_chain[q, e], t_t[q, l // 2 % 2, l % 2, h, :], rhs[q, l % 2, e], start=True, stop=True)
                    last.then_inc(s["err_psum"], 1)
                n, l, live = on(base, j, LAG_OUT)
                if not live:
                    gram_ready(base, j)
                if live:
                    wait(pe, s["o_done"], n + 1)
                    wait(pe, s["ot_lo"], n)
                    for kb in range(KB):
                        if kb == KB - 1:
                            gram_ready(base, j)
                        last = pe.transpose(ps_ot[:, P * kb:P * kb + P], o_g[:, l % 2, P * kb:P * kb + P], k["ident"][:, :])
                    last.then_inc(s["ot_psum"], 1)
                n, l, live = on(base, j, LAG_GRAM)
                if live:
                    for h, q, e in blocks():
                        last = pe.matmul(ps_gram[q, e], key_t[q, l, h, :], key_t[q, l, h, :], start=True, stop=True)
                    last.then_inc(s["gram_psum"], 1)
                if not live:
                    update_ready(base, j)
                if live:
                    if isinstance(n, int) and n == 0:
                        pe.wait_ge(s["first_gate"], 1)
                    wait(pe, s["gates_done"], n + 1)
                    wait(pe, s["gexp_done"], upto(n + 2))
                    wait(pe, s["gate_done"], n)
                    pe.matmul(ps_g[:, 2 * H:3 * H], k["carry"][:, :], gates[:, (l - 1) % 8, H:2 * H], start=True, stop=False)
                    update_ready(base, j)
                    pe.matmul(ps_g[:, 2 * H:3 * H], k["shift"][:, :], gates[:, l, H:2 * H],
                              start=False, stop=True).then_inc(s["gate_psum"], 1)
                n, l, live = on(base, j, 0)
                if live:
                    for h, q, e in blocks():
                        last = pe.matmul(ps_s[q, e], key_b[q, l, e], err[q, l % 2, e],
                                         start=(isinstance(n, int) and n == 0 and h == 0), stop=True, skip_group_check=True)
                    last.then_inc(s["s_psum"], 1)
                n, l, live = on(base, j, LAG_OUT)
                if live:
                    wait(pe, s["ot_lo"], n + 1)
                    wait(pe, s["yn_done"], n)
                    for i in range(3 * KB):
                        if i == 3 * KB - 1:
                            chain_ready(base, j + 1)
                        kb, (a, w) = i // 3, PARTS3[i % 3]
                        last = pe.matmul(ps_y[:, :], ot[:, l % 2, a, kb, :], k["wo"][:, w, kb, :],
                                         start=(i == 0), stop=(i == 3 * KB - 1))
                    last.then_inc(s["y_psum"], 1)
            run(pe, step)


def feed_forward(nc, io, k):
    with ExitStack() as ctx:
        def sb(name, shape, dt=F32):
            return ctx.enter_context(nc.sbuf_tensor(name, shape, dt))

        def sem(name):
            return ctx.enter_context(nc.semaphore(name))

        top = sb("f_top", [P, 1])
        top_all = sb("f_top_all", [P, 1])
        inv = sb("f_inv", [P, 1])
        q_scale = sb("q_scale", [P, 1])
        gb = sb("f_gb", [P, 2 * KB])
        unit = sb("f_unit", [P, 1])
        down = sb("f_down", [P, 1])
        y_eps = sb("y_eps", [P, 1])
        unit_t = sb("f_unit_t", [P, 1])
        x1 = sb("f_x1", [P, 4, G, D])
        sc = sb("f_sc", [P, 2, G, 2])
        z = sb("f_z", [P, 2, G, D])
        u = sb("f_u", [P, KB, G * P])
        uc = sb("f_uc", [P, KB, G * P])
        xq = sb("f_xq", [P, 2, 2, KB, G * P], F16)
        raw = sb("f_raw", [P, G, 6])
        mv = sb("f_mv", [P, 2, G, 2])
        veps = sb("f_veps", [P, G])
        neg = sb("f_neg", [P, G])
        ysc = sb("f_ysc", [P, 2, G, 2])
        yn = sb("f_yn", [P, G, D])
        res = sb("f_res", [P, 2, G, D])
        ps_z = [ctx.enter_context(nc.psum_tensor(f"ps_z{i}", [P, G * P], F32)) for i in range(KB)]
        ps_f = [ctx.enter_context(nc.psum_tensor(f"ps_f{i}", [P, D], F32)) for i in range(G)]

        loaded = [sem(f"f_loaded{i}") for i in range(4)]
        stored = [sem(f"f_stored{i}") for i in range(2)]
        names = """f_rowtop f_top f_inv f_scaled f_gb f_unit f_sc f_z f_zt f_u f_clip f_hi f_lo f_y
            f_sums f_stats f_veps f_rstd f_ysc f_yn f_res""".split()
        s = {n: sem(n) for n in names}

        def run(eng, step):
            for j in range(-1, 4):
                step(None, j)
            with eng.Fori(1, NG // 4 - 1) as base:
                for i in range(4):
                    step(base, i)
            for j in range(NG - 4, NG + 1):
                step(None, j)

        def on(base, step, lag):
            g = step + lag if base is None else base * 4 + (step + lag)
            return g, (step + lag) % 4, not isinstance(g, int) or 0 <= g < NG

        def wait(eng, semaphore, count):
            if not isinstance(count, int) or count > 0:
                eng.wait_ge(semaphore, count)

        block = ctx.enter_context(nc.Block())

        @block.sync
        def _(sp):
            def step(base, j):
                g, r, live = on(base, j, 1)
                if live:
                    wait(sp, s["f_res"], (g - 3) * G)
                    sp.dma_start(x1[:, r, :, :], k["x1_dram"][bass.ds(g * G, G), :, :].rearrange("g p d -> p g d"))\
                      .then_inc(loaded[r], 16)
                g, r, live = on(base, j, -1)
                if live:
                    sp.wait_ge(s["f_res"], g * G + G)
                    for b in range(B):
                        dst = io["out"][b, bass.ds(g * G * C, G * C), :].rearrange("(g t) d -> t g d", g=G)
                        sp.dma_start(dst, res[C * b:C * b + C, r % 2, :, :]).then_inc(stored[r % 2], 16)
            run(sp, step)
            for r in range(2):
                sp.wait_ge(stored[r], 16 * B * NG // 2)

        @block.gpsimd
        def _(pool):
            pool.wait_ge(s["f_rowtop"], 1)
            pool.partition_all_reduce(top_all[:, :], top[:, :], P, RMAX).then_inc(s["f_top"], 1)
            pool.wait_ge(s["f_unit"], 3)

            def step(base, j):
                g, r, live = on(base, j, -1)
                if not live:
                    return
                pool.wait_ge(s["f_stats"], g * G + G)
                wait(pool, s["f_yn"], (g - 1) * G)
                pool.tensor_tensor(veps[:, :], mv[:, r % 2, :, 1], y_eps[:, 0:1].to_broadcast([P, G]), ALU.add).then_inc(s["f_veps"], 1)
                pool.tensor_tensor(neg[:, :], mv[:, r % 2, :, 0], k["minus_one"][:, 0:1].to_broadcast([P, G]), ALU.mult).then_inc(s["f_veps"], 1)
                pool.wait_ge(s["f_veps"], g * 2 + 2)
                pool.tensor_tensor(ysc[:, r % 2, :, 0], veps[:, :], k["neg_half"][:, 0:1].to_broadcast([P, G]), ALU.pow).then_inc(s["f_rstd"], 1)
                pool.wait_ge(s["f_rstd"], g + 1)
                pool.tensor_tensor(ysc[:, r % 2, :, 1], neg[:, :], ysc[:, r % 2, :, 0], ALU.mult).then_inc(s["f_ysc"], 1)
                for i in range(G):
                    pool.wait_ge(s["f_yn"], g * G + (i + 1))
                    if i == 0 and (not isinstance(g, int) or g >= 2):
                        pool.wait_ge(stored[r % 2], (g - r % 2) * (8 * B))
                    pool.tensor_tensor(res[:, r % 2, i, :], yn[:, i, :], x1[:, r, i, :], ALU.add).then_inc(s["f_res"], 1)
            run(pool, step)

        @block.scalar
        def _(act):
            act.wait_ge(s["f_gb"], 1)

            def step(base, j):
                g, r, live = on(base, j, 0)
                if live:
                    act.wait_ge(s["f_clip"], g + 1)
                    wait(act, s["f_y"], (g - 1) * G)
                    nc.scalar.activation(xq[:, r % 2, 0, :, :], uc[:, :, :], ACT.Copy).then_inc(s["f_hi"], 1)
                g, r, live = on(base, j, 1)
                if live:
                    for kb in range(KB):
                        act.wait_ge(s["f_zt"], g * KB + (kb + 1))
                        if kb == 0:
                            wait(act, s["f_clip"], g)
                        nc.scalar.activation(u[:, kb, :], ps_z[kb][:, :], ACT.Identity, scale=gb[:, kb:kb + 1],
                                             bias=gb[:, KB + kb:KB + kb + 1]).then_inc(s["f_u"], 1)
                g, r, live = on(base, j, -1)
                if live:
                    for i in range(G):
                        if i == 0:
                            act.wait_ge(s["f_ysc"], g + 1)
                        wait(act, s["f_res"], (g - 1) * G + (i + 1))
                        nc.scalar.activation(yn[:, i, :], ps_f[i][:, :], ACT.Identity, scale=ysc[:, r % 2, i, 0:1],
                                             bias=ysc[:, r % 2, i, 1:2]).then_inc(s["f_yn"], 1)
            run(act, step)

        @block.vector
        def _(dve):
            dve.tensor_reduce(top[:, :], k["row_max"][:, :], AX_X, ALU.max).then_inc(s["f_rowtop"], 1)
            dve.wait_ge(s["f_top"], 1)
            dve.reciprocal(inv[:, :], top_all[:, :]).then_inc(s["f_inv"], 1)
            dve.wait_ge(s["f_inv"], 1)
            dve.tensor_scalar(q_scale[:, :], inv[:, :], QB, None, ALU.mult).then_inc(s["f_scaled"], 1)
            dve.tensor_tensor(unit_t[:, :], top_all[:, :], k["w_mean"][:, :], ALU.mult).then_inc(s["f_scaled"], 1)
            dve.wait_ge(s["f_scaled"], 2)
            dve.tensor_scalar(gb[:, :], k["gb_cols"][:, :], q_scale[:, 0:1], None, ALU.mult).then_inc(s["f_gb"], 1)
            dve.tensor_scalar(unit[:, :], unit_t[:, :], 1.0 / QB, None, ALU.mult).then_inc(s["f_unit"], 1)
            dve.wait_ge(s["f_unit"], 1)
            dve.reciprocal(down[:, :], unit[:, :]).then_inc(s["f_unit"], 1)
            dve.wait_ge(s["f_unit"], 2)
            dve.scalar_tensor_tensor(out=y_eps[:, :], in0=down[:, :], scalar=LN_EPS, in1=down[:, :],
                                     op0=ALU.mult, op1=ALU.mult).then_inc(s["f_unit"], 1)

            def step(base, j):
                g, r, live = on(base, j, -1)
                if live:
                    wait(dve, s["f_ysc"], g - 1)
                    for i in range(G):
                        dve.wait_ge(s["f_y"], g * G + (i + 1))
                        wait(dve, s["f_stats"], (g - 1) * G + (i + 1))
                        if i > 0:
                            dve.wait_ge(s["f_sums"], g * G + i)
                        dve.bn_stats(raw[:, i, :], ps_f[i][:, :]).then_inc(s["f_sums"], 1)
                        if i > 0:
                            dve.bn_aggr(mv[:, r % 2, i - 1, :], raw[:, i - 1, :]).then_inc(s["f_stats"], 1)
                    dve.wait_ge(s["f_sums"], g * G + G)
                g, r, live = on(base, j, 1)
                if live:
                    wait(dve, s["f_z"], (g - 1) * G)
                    dve.tensor_copy(sc[:, r % 2, :, :].rearrange("p g c -> p (g c)"),
                                    k["z_scale"][:, bass.ds(g * (2 * G), 2 * G)]).then_inc(s["f_sc"], 1)
                    dve.wait_ge(loaded[r], (g - r) * 4 + 16)
                    wait(dve, s["f_zt"], (g - 1) * KB)
                    dve.wait_ge(s["f_sc"], g + 1)
                    for i in range(G):
                        dve.tensor_scalar(z[:, r % 2, i, :], x1[:, r, i, :], sc[:, r % 2, i, 0:1], sc[:, r % 2, i, 1:2],
                                          ALU.mult, ALU.add).then_inc(s["f_z"], 1)
                g, r, live = on(base, j, -1)
                if live:
                    dve.bn_aggr(mv[:, r % 2, G - 1, :], raw[:, G - 1, :]).then_inc(s["f_stats"], 1)
                g, r, live = on(base, j, 0)
                if live:
                    dve.wait_ge(s["f_u"], g * KB + KB)
                    wait(dve, s["f_lo"], g)
                    wait(dve, s["f_hi"], g)
                    dve.tensor_scalar(uc[:, :, :], u[:, :, :], QB - Q_EPS, -(QB - Q_EPS), ALU.min, ALU.max).then_inc(s["f_clip"], 1)
                    dve.wait_ge(s["f_hi"], g + 1)
                    wait(dve, s["f_y"], (g - 1) * G)
                    dve.tensor_tensor(xq[:, r % 2, 1, :, :], uc[:, :, :], xq[:, r % 2, 0, :, :], ALU.subtract).then_inc(s["f_lo"], 1)
            run(dve, step)

        @block.tensor
        def _(pe):
            def step(base, j):
                g, r, live = on(base, j, 1)
                if live:
                    pe.wait_ge(s["f_z"], g * G + G)
                    for kb in range(KB):
                        wait(pe, s["f_u"], (g - 1) * KB + (kb + 1))
                        for i in range(G):
                            last = pe.transpose(ps_z[kb][:, P * i:P * i + P], z[:, r % 2, i, P * kb:P * kb + P], k["ident"][:, :])
                        last.then_inc(s["f_zt"], 1)
                g, r, live = on(base, j, 0)
                if live:
                    pe.wait_ge(s["f_lo"], g + 1)
                    for i in range(G):
                        wait(pe, s["f_yn"], (g - 1) * G + (i + 1))
                        for m in range(2 * KB):
                            kb, a = m // 2, m % 2
                            last = pe.matmul(ps_f[i][:, :], xq[:, r % 2, a, kb, P * i:P * i + P], k["wq"][:, kb, :],
                                             start=(m == 0), stop=(m == 2 * KB - 1))
                        last.then_inc(s["f_y"], 1)
            run(pe, step)


def build(nc, x, Wv, Wo, Wg, Wb, Wf, gamma, beta, out):
    io = dict(x=x, Wv=Wv, Wo=Wo, Wg=Wg, Wb=Wb, Wf=Wf, gamma=gamma, beta=beta, out=out)
    with ExitStack() as ctx:
        def sb(name, shape, dt=F32):
            return ctx.enter_context(nc.sbuf_tensor(name, shape, dt))
        k = dict(
            ident=sb("ident", [P, P]), shift=sb("shift", [P, P]), carry=sb("carry", [P, P]), neg_mask=sb("neg_mask", [P, C]), neg_half=sb("neg_half", [P, 1]),
            minus_one=sb("minus_one", [P, 1]), ln_eps=sb("ln_eps", [P, 1]), z_gain=sb("z_gain", [P, 1]), z_eps=sb("z_eps", [P, 1]),
            rn_bias=sb("rn_bias", [P, 1]),
            wv=sb("wv", [P, 2, KB, D], F16), wo=sb("wo", [P, 2, KB, D], F16),
            wgb=sb("wgb", [P, 2, KB, 2 * H], F16), wq=sb("wq", [P, KB, D], F16),
            w_mean=sb("w_mean", [P, 1]), attn_eps=sb("attn_eps", [P, 1]), gate_unit=sb("gate_unit", [P, 1]),
            gamma_bc=sb("gamma_bc", [P, D]), beta_bc=sb("beta_bc", [P, D]), gb_cols=sb("gb_cols", [P, 2 * KB]),
            z_scale=sb("z_scale", [P, 2 * NT]),
            row_max=sb("row_max", [P, NT]),
            x1_dram=nc.dram_tensor("x1_scratch", (NT, P, D), F32).ap(),
        )
        setup(nc, io, k)
        attention(nc, io, k)
        feed_forward(nc, io, k)


_INS = ["L0_attn_x", "L0_attn_Wv", "L0_attn_Wo", "L0_attn_Wg", "L0_attn_Wb", "L0_ffn_weight", "L0_ffn_ln_gamma", "L0_ffn_ln_beta"]


def kernel(**inputs):
    import numpy as _np
    import concourse.bacc as _bacc
    from concourse import mybir as _mybir
    from concourse.bass_utils import run_bass_kernel_spmd as _run

    nc = _bacc.Bacc("TRN2", target_bir_lowering=False, num_devices=1)
    arrays, args = {}, []
    for name in _INS:
        a = _np.ascontiguousarray(inputs[name])
        arrays[f"in_{name}"] = a
        args.append(nc.dram_tensor(f"in_{name}", a.shape, _mybir.dt.from_np(a.dtype), kind="ExternalInput").ap())
    out = nc.dram_tensor("out_0", (B, T, D), F32, kind="ExternalOutput").ap()
    build(nc, *args, out)
    r = _run(nc, [arrays], core_ids=[0])
    return r.results[0]["out_0"]
```
